# Optimizing a Trainium2 kernel written in Bass

```python
import numpy as np
import jax
import jax.numpy as jnp

def _softmax(x, axis=-1):
    return jax.nn.softmax(x, axis=axis)
def _gelu(x):
    return jax.nn.gelu(x, approximate=True)
def _silu(x):
    return jax.nn.silu(x)
def _sigmoid(x):
    return jax.nn.sigmoid(x)
def _layernorm(x, axis=-1, eps=1e-5):
    m = jnp.mean(x, axis=axis, keepdims=True)
    v = jnp.var(x, axis=axis, keepdims=True)
    return (x - m) / jnp.sqrt(v + eps)
def _scatter_add(tgt, idx, src, axis=0):
    return tgt.at[idx].add(src)
def _segment_sum(src, seg, n):
    return jax.ops.segment_sum(src, seg, n)

kernel_name = 'mk_rec_standalone_d1_rec_89bba4'

def setup_inputs(seed: int = 0):
    np.random.seed(seed)
    _w = jnp.asarray
    def _rec_inputs():
        import jax
        import jax.numpy as jnp
        _rk = jax.random.key(seed)
        r_x = -0.000153849 + 1.00027 * jax.random.normal(jax.random.fold_in(_rk, 1), (4096, 24, 64), jnp.float32)
        return r_x
    r_x = _rec_inputs()
    def _L0_rec_setup():
        import jax, jax.numpy as jnp
        import numpy as np
        import itertools
        FIELD_NUM = 24

        def _pair_idx(field_num):
            pairs = np.array(list(itertools.combinations(range(field_num), 2)), dtype=np.int32)
            return (pairs[:, 0], pairs[:, 1])
        key = jax.random.key(seed)
        k1, k2 = jax.random.split(key)
        B, F, E = (4096, FIELD_NUM, 64)
        P = F * (F - 1) // 2
        x = jax.random.normal(k1, (B, F, E), dtype=jnp.float32)
        W = jax.random.normal(k2, (P, E, E), dtype=jnp.float32) * 0.05
        return {'x': x, 'W': W}
    _L0_rec_all = _L0_rec_setup()
    _L0_rec_in = {k: v for k, v in _L0_rec_all.items() if k in ('W', )}
    del _L0_rec_all

    return {
        "r_x": r_x,
        "L0_rec_W": _L0_rec_in["W"],
    }

def reference(r_x, L0_rec_W):
    import jax
    import jax.numpy as jnp
    def _L0_rec_ref(x, W):
        import jax, jax.numpy as jnp
        import numpy as np
        import itertools
        FIELD_NUM = 24

        def _pair_idx(field_num):
            pairs = np.array(list(itertools.combinations(range(field_num), 2)), dtype=np.int32)
            return (pairs[:, 0], pairs[:, 1])
        i_idx, j_idx = _pair_idx(x.shape[1])
        xi = x[:, i_idx, :]
        xj = x[:, j_idx, :]
        return jnp.einsum('bpe,pef->bpf', xi, W) * xj

    y = _L0_rec_ref(r_x, L0_rec_W)
    return y


_drawn_inputs = setup_inputs


def setup_inputs(seed=0):
    import zlib

    import numpy as np

    out = dict(_drawn_inputs(seed))
    spreads = {}
    factors = {}
    for name, (base, spread) in spreads.items():
        noise = np.random.default_rng([zlib.crc32(name.encode()), seed]).standard_normal(out[name].shape)
        drawn = base * np.exp(spread * noise) if base else spread * noise
        out[name] = jnp.asarray(drawn.astype(out[name].dtype))
    for name, factor in factors.items():
        out[name] = (out[name] * factor).astype(out[name].dtype)
    return out
```

```python
import concourse.bass as bass
from concourse import mybir
from contextlib import ExitStack

P = 128
BANK = 512
SLOT_BANKS = 2
SLOTS = 4


def pairwise_bilinear(nc, x, w, out):
    fp32 = mybir.dt.float32
    ALU = mybir.AluOpType
    B, F, E = x.shape
    TILES = B // P
    LAST = TILES // 2 - 1
    PAIRS = F * (F - 1) // 2
    FIRST_PAIR = [i * (2 * F - i - 1) // 2 for i in range(F)]
    BANK_PAIRS = BANK // E
    SLOT_PAIRS = SLOT_BANKS * BANK_PAIRS
    COUPLES = F // 2

    def partners(i):
        return F - 1 - i

    w_col = [E * sum(partners(h) for h in range(i % 2, i, 2)) for i in range(F)]
    W_COLS = E * sum(partners(h) for h in range(0, F, 2))

    TRANSPOSES = [(0, 8), (8, COUPLES - 8)]
    TRANSPOSE_AFTER = 4
    steps = []
    for k in range(COUPLES):
        halves = []
        for i in (2 * k, 2 * k + 1):
            n = -(-partners(i) // SLOT_PAIRS)
            cut = [partners(i) * c // n for c in range(n + 1)] if n else [0]
            halves.append([(k, i, a, b - a) for a, b in zip(cut, cut[1:])])
        while halves[0] or halves[1]:
            step = [half.pop(0) for half in halves if half]
            steps.append(sorted(step, key=lambda piece: -(-piece[3] // BANK_PAIRS)))
        if k == TRANSPOSE_AFTER:
            steps.append("transposes")
    order = []
    products = []
    for step in steps:
        if step == "transposes":
            order += [("transpose", n) for n in range(len(TRANSPOSES))]
        else:
            for piece in step:
                order.append(("product", len(products)))
                products.append(piece)
    USES, PRODUCTS, EVACS = len(order), len(products), len(TRANSPOSES)
    assert USES % SLOTS == 0

    CHUNKS = [(0, 1), (1, 2), (2, 3), (3, 4), (4, 5), (5, 7), (7, COUPLES)]
    chunk_of = {k: c for c, (k0, k1) in enumerate(CHUNKS) for k in range(k0, k1)}
    chunk_end = [max(n for n, p in enumerate(products) if p[0] < k1) + 1 for _, k1 in CHUNKS]
    chunk_cols = [(FIRST_PAIR[2 * k0] * E, (FIRST_PAIR[2 * k1] if k1 < COUPLES else PAIRS) * E)
                  for k0, k1 in CHUNKS]

    x_tiles = x.rearrange("(c h p) f e -> c h p (f e)", h=2, p=P)
    out_tiles = out.rearrange("(c h p) q e -> c h p (q e)", h=2, p=P)

    with ExitStack() as ctx:
        def sb(name, shape):
            return ctx.enter_context(nc.sbuf_tensor(name, shape, fp32))

        def sem(name):
            return ctx.enter_context(nc.semaphore(name))

        w_sb = sb("w_sb", [P, W_COLS])
        x_sb = [sb(f"x_sb{h}", [P, F * E]) for h in range(2)]
        xt_sb = [sb(f"xt_sb{h}", [P, COUPLES * P]) for h in range(2)]
        out_sb = [sb(f"out_sb{h}", [P, PAIRS * E]) for h in range(2)]
        identity = sb("identity", [P, P])
        slots = [ctx.enter_context(nc.psum_tensor(f"slot{s}", [P, SLOT_BANKS * BANK], fp32)) for s in range(SLOTS)]

        zeroed = sem("zeroed")
        identity_ready = sem("identity_ready")
        w_loaded = [sem(f"w_loaded{k}") for k in range(COUPLES)]
        x_loaded = [sem(f"x_loaded{h}") for h in range(2)]
        transposes_ready = sem("transposes_ready")
        xt_ready = sem("xt_ready")
        product_ready = sem("product_ready")
        scaled = sem("scaled")
        stored = [[sem(f"stored{h}_{c}") for c in range(len(CHUNKS))] for h in range(2)]

        block = ctx.enter_context(nc.Block())

        def all_couples(eng, couple_of_tiles):
            couple_of_tiles(0, True, False)
            with eng.Fori(1, LAST) as c:
                couple_of_tiles(c, False, False)
            couple_of_tiles(LAST, False, True)

        @block.gpsimd
        def _(pool):
            nc.gpsimd.memset(identity[:], 0.0).then_inc(zeroed, 1)
            pool.wait_ge(zeroed, 1)
            nc.gpsimd.affine_select(out=identity[:], in_=identity[:], compare_op=ALU.not_equal, fill=1.0, base=0,
                                    pattern=[[-1, P]], channel_multiplier=1).then_inc(identity_ready, 1)

        @block.sync
        def _(sp):
            sp.dma_start(x_sb[0][:], x_tiles[0, 0]).then_inc(x_loaded[0], 16)
            for i in range(F - 1):
                rows = slice(E * (i % 2), E * (i % 2) + E)
                cols = slice(w_col[i], w_col[i] + partners(i) * E)
                sp.dma_start(w_sb[rows, cols].rearrange("e (q f) -> e q f", f=E),
                             w[FIRST_PAIR[i]:FIRST_PAIR[i] + partners(i)].rearrange("q e f -> e q f")
                             ).then_inc(w_loaded[i // 2], 16)

            def store(c, first, last):
                for h in range(2):
                    for n, (a, b) in enumerate(chunk_cols):
                        sp.wait_ge(scaled, (c * 2 + h) * PRODUCTS + chunk_end[n])
                        sp.dma_start(out_tiles[c, h, :, a:b], out_sb[h][:, a:b]).then_inc(stored[h][n], 16)

            all_couples(sp, store)
            for h in range(2):
                for n in range(len(CHUNKS)):
                    sp.wait_ge(stored[h][n], 16 * (TILES // 2))

        @block.scalar
        def _(act):
            act.dma_start(x_sb[1][:], x_tiles[0, 1]).then_inc(x_loaded[1], 16)

            def evacuate(c, h):
                for n, (k0, kn) in enumerate(TRANSPOSES):
                    use = order.index(("transpose", n))
                    act.wait_ge(transposes_ready, (c * 2 + h) * EVACS + n + 1)
                    nc.scalar.copy(xt_sb[h][:, k0 * P:(k0 + kn) * P],
                                   slots[use % SLOTS][:, 0:kn * P]).then_inc(xt_ready, 1)

            def x_ahead(c, first, last):
                for h in range(2):
                    if not (last and h == 1):
                        evacuate(c + h, 1 - h)
                    if not last:
                        act.wait_ge(scaled, (c * 2 + h + 1) * PRODUCTS)
                        act.dma_start(x_sb[h][:], x_tiles[c + 1, h]).then_inc(x_loaded[h], 16)

            evacuate(0, 0)
            all_couples(act, x_ahead)

        @block.tensor
        def _(pe):
            def transpose(c, h, n):
                use = order.index(("transpose", n))
                k0, kn = TRANSPOSES[n]
                for k in range(k0, k0 + kn):
                    last = nc.tensor.transpose(slots[use % SLOTS][:, (k - k0) * P:(k - k0 + 1) * P],
                                               x_sb[h][:, k * P:(k + 1) * P], identity[:])
                last.then_inc(transposes_ready, 1)

            def slot_free(use, c, h, first, last=False):
                tile = c * 2 + h
                before = use - SLOTS
                if last and h == 1 and order[before][0] == "transpose":
                    before -= SLOTS
                if before < 0:
                    if first and h == 0:
                        return
                    tile, before = tile - 1, before + USES
                kind, n = order[before]
                if kind == "product":
                    pe.wait_ge(scaled, tile * PRODUCTS + n + 1)
                else:
                    pe.wait_ge(xt_ready, (tile + 1) * EVACS + n + 1)

            def tile_products(c, h, first, last):
                pe.wait_ge(xt_ready, (c * 2 + h + 1) * EVACS)
                use = 0
                for step in steps:
                    if step == "transposes":
                        if last and h == 1:
                            use += EVACS
                            continue
                        pe.wait_ge(x_loaded[1 - h], 16 * (c + h + 1))
                        for n in range(EVACS):
                            slot_free(use, c, h, first)
                            transpose(c + h, 1 - h, n)
                            use += 1
                        continue
                    if first and h == 0 and step[0][2] == 0:
                        k = step[0][0]
                        pe.wait_ge(w_loaded[k], 16 * sum(i < F - 1 for i in (2 * k, 2 * k + 1)))
                    for n in range(len(step)):
                        slot_free(use + n, c, h, first, last)
                    for bank in range(SLOT_BANKS):
                        for n, (k, i, j0, jn) in enumerate(step):
                            a, b = bank * BANK_PAIRS, min((bank + 1) * BANK_PAIRS, jn)
                            if a >= b:
                                continue
                            rows = slice(E * (i % 2), E * (i % 2) + E)
                            done = nc.tensor.matmul(slots[(use + n) % SLOTS][:, a * E:b * E],
                                                    xt_sb[h][rows, k * P:(k + 1) * P],
                                                    w_sb[rows, w_col[i] + (j0 + a) * E:w_col[i] + (j0 + b) * E],
                                                    start=True, stop=True)
                            if b == jn:
                                done.then_inc(product_ready, 1)
                    use += len(step)

            pe.wait_ge(identity_ready, 1)
            pe.wait_ge(x_loaded[0], 16)
            for n in range(EVACS):
                transpose(0, 0, n)

            def couple(c, first, last):
                for h in range(2):
                    tile_products(c, h, first, last)

            all_couples(pe, couple)

        @block.vector
        def _(dve):
            def couple(c, first, last):
                for h in range(2):
                    dve.wait_ge(x_loaded[h], 16 * (c + 1))
                    for n, (k, i, j0, jn) in enumerate(products):
                        chunk = chunk_of[k]
                        if not first and (n == 0 or chunk_of[products[n - 1][0]] != chunk):
                            dve.wait_ge(stored[h][chunk], 16 * c)
                        dve.wait_ge(product_ready, (c * 2 + h) * PRODUCTS + n + 1)
                        use = order.index(("product", n))
                        o = (FIRST_PAIR[i] + j0) * E
                        xj = (i + 1 + j0) * E
                        nc.vector.tensor_tensor(out_sb[h][:, o:o + jn * E], slots[use % SLOTS][:, 0:jn * E],
                                                x_sb[h][:, xj:xj + jn * E], ALU.mult).then_inc(scaled, 1)

            all_couples(dve, couple)


def kernel(r_x, L0_rec_W):
    import numpy as np
    import concourse.bacc as bacc
    from concourse.bass_utils import run_bass_kernel_spmd

    x = np.ascontiguousarray(r_x)
    w = np.ascontiguousarray(L0_rec_W)
    B, F, E = x.shape
    fp32 = mybir.dt.float32
    nc = bacc.Bacc("TRN2", target_bir_lowering=False, num_devices=1)
    x_dram = nc.dram_tensor("x_dram", x.shape, fp32, kind="ExternalInput").ap()
    w_dram = nc.dram_tensor("w_dram", w.shape, fp32, kind="ExternalInput").ap()
    out_dram = nc.dram_tensor("out_dram", (B, F * (F - 1) // 2, E), fp32, kind="ExternalOutput").ap()
    pairwise_bilinear(nc, x_dram, w_dram, out_dram)
    result = run_bass_kernel_spmd(nc, [{"x_dram": x, "w_dram": w}], core_ids=[0])
    return result.results[0]["out_dram"]
```

```python
import concourse.bass as bass
from concourse import mybir
from contextlib import ExitStack

P = 128
BANK = 512
SLOT_BANKS = 2
SLOTS = 4


def pairwise_bilinear(nc, x, w, out):
    fp32 = mybir.dt.float32
    fp32r = mybir.dt.float32r
    ALU = mybir.AluOpType
    B, F, E = x.shape
    TILES = B // P
    LAST = TILES // 2 - 1
    FIELDS = F - 1
    PAIRS = F * (F - 1) // 2
    FIRST_PAIR = [i * (2 * F - i - 1) // 2 for i in range(F)]
    BANK_PAIRS = BANK // E
    SLOT_PAIRS = SLOT_BANKS * BANK_PAIRS

    def pair_cols(i0, i1):
        return slice(FIRST_PAIR[i0] * E, FIRST_PAIR[i1] * E)

    products = []
    for i in range(FIELDS):
        partners = F - 1 - i
        n = -(-partners // SLOT_PAIRS)
        cut = [partners * c // n for c in range(n + 1)]
        products += [(i, a, b - a) for a, b in zip(cut, cut[1:])]
    PRODUCTS = len(products)

    GROUP_FIELDS = SLOT_BANKS * BANK // (2 * P)
    GROUPS = [(f, min(f + GROUP_FIELDS, FIELDS)) for f in range(0, FIELDS, GROUP_FIELDS)]
    AHEAD_AFTER = [9, 11, 13, 15, 19, FIELDS - 1]
    OWN_BEFORE = [0, 1, 2, 3, 4, 4]

    def plan(first, last):
        uses = []
        for i in range(FIELDS):
            if first:
                uses += [("own", g) for g in range(len(GROUPS)) if OWN_BEFORE[g] == i]
            uses += [("product", n) for n, piece in enumerate(products) if piece[0] == i]
            if not last:
                uses += [("ahead", g) for g in range(len(GROUPS)) if AHEAD_AFTER[g] == i]
        skew = -len(uses) if first else 0
        holder = {}
        if not first:
            for u, (kind, n) in enumerate(STEADY_USES):
                holder[u % SLOTS] = (kind, n, -1)
        planned = []
        for u, (kind, n) in enumerate(uses):
            slot = (u + skew) % SLOTS
            planned.append((kind, n, slot, holder.get(slot)))
            holder[slot] = (kind, n, 0)
        return planned

    STEADY_USES = [(kind, n) for kind, n, _, _ in [
        u for i in range(FIELDS) for u in
        [("product", n, 0, 0) for n, piece in enumerate(products) if piece[0] == i]
        + [("ahead", g, 0, 0) for g in range(len(GROUPS)) if AHEAD_AFTER[g] == i]]]
    assert len(STEADY_USES) % SLOTS == 0

    CHUNKS = [(0, 2), (2, 4), (4, 6), (6, 8), (8, 10), (10, 12), (12, 15), (15, FIELDS)]
    chunk_start = [min(n for n, piece in enumerate(products) if piece[0] >= i0) for i0, _ in CHUNKS]
    chunk_end = chunk_start[1:] + [PRODUCTS]
    W_PARTS = [(0, 1), (1, 2)] + CHUNKS[1:]
    W_LOW_ON_VECTOR = 3

    x_tiles = x.rearrange("(c h p) f e -> c h p (f e)", h=2, p=P)
    out_tiles = out.rearrange("(c h p) q e -> c h p (q e)", h=2, p=P)
    w_cols = w.rearrange("e q f -> e (q f)")

    with ExitStack() as ctx:
        def sb(name, shape, dt=fp32):
            return ctx.enter_context(nc.sbuf_tensor(name, shape, dt))

        def sem(name):
            return ctx.enter_context(nc.semaphore(name))

        w_split = sb("w_split", [P, PAIRS * E], fp32r)
        x_sb = [sb(f"x_sb{h}", [P, F * E]) for h in range(2)]
        x_split = sb("x_split", [P, FIELDS, 3, E], fp32r)
        xt_sb = sb("xt_sb", [P, FIELDS, 2, P], fp32r)
        out_sb = sb("out_sb", [P, PAIRS * E])
        identity = sb("identity", [P, P])
        slots = [ctx.enter_context(nc.psum_tensor(f"slot{s}", [P, SLOT_BANKS * BANK], fp32)) for s in range(SLOTS)]

        zeroed = sem("zeroed")
        identity_ready = sem("identity_ready")
        w_loaded = [sem(f"w_loaded{n}") for n in range(len(W_PARTS))]
        w_high_ready = sem("w_high_ready")
        w_ready = [sem(f"w_ready{n}") for n in range(len(W_PARTS))]
        x_loaded = [sem(f"x_loaded{h}") for h in range(2)]
        x_high_ready = sem("x_high_ready")
        x_split_ready = sem("x_split_ready")
        transposes_ready = sem("transposes_ready")
        xt_ready = sem("xt_ready")
        product_ready = sem("product_ready")
        scaled = sem("scaled")
        stored = [sem(f"stored{c}") for c in range(len(CHUNKS))]

        block = ctx.enter_context(nc.Block())

        X0_PARTS = [GROUPS[0], (GROUPS[0][1], FIELDS)]

        def splits(tile):
            return tile + len(X0_PARTS)

        def all_couples(eng, couple_of_tiles):
            couple_of_tiles(0, True, False)
            with eng.Fori(1, LAST) as c:
                couple_of_tiles(c, False, False)
            couple_of_tiles(LAST, False, True)

        def plan_of(h, first, last):
            return plan(first and h == 0, last and h == 1)

        @block.sync
        def _(sp):
            for n, (i0, i1) in enumerate(W_PARTS):
                cols = pair_cols(i0, i1)
                sp.dma_start(out_sb[0:E, cols], w_cols[:, cols]).then_inc(w_loaded[n], 16)

            def store(c, first, last):
                for h in range(2):
                    for n, (i0, i1) in enumerate(CHUNKS):
                        sp.wait_ge(scaled, (c * 2 + h) * PRODUCTS + chunk_end[n])
                        cols = pair_cols(i0, i1)
                        sp.dma_start(out_tiles[c, h, :, cols], out_sb[:, cols]).then_inc(stored[n], 16)

            all_couples(sp, store)
            for n in range(len(CHUNKS)):
                sp.wait_ge(stored[n], 16 * TILES)

        @block.scalar
        def _(act):
            act.dma_start(x_sb[0][:], x_tiles[0, 0]).then_inc(x_loaded[0], 16)
            act.dma_start(x_sb[1][:], x_tiles[0, 1]).then_inc(x_loaded[1], 16)

            def x_high(h, i0, i1):
                n = i1 - i0
                nc.scalar.copy(x_split[:, i0:i1, 0:3:2, :],
                               x_sb[h][:, i0 * E:i1 * E].rearrange("p (i o e) -> p i o e", o=1, e=E)
                               .to_broadcast([P, n, 2, E])).then_inc(x_high_ready, 1)

            def w_high(n):
                act.wait_ge(w_loaded[n], 16)
                cols = pair_cols(*W_PARTS[n])
                nc.scalar.copy(w_split[0:E, cols], out_sb[0:E, cols]).then_inc(w_high_ready, 1)

            def evacuate(tile, g, slot):
                i0, i1 = GROUPS[g]
                act.wait_ge(transposes_ready, tile * len(GROUPS) + g + 1)
                nc.scalar.copy(xt_sb[:, i0:i1].rearrange("p i v b -> p (i v b)"),
                               slots[slot][:, 0:(i1 - i0) * 2 * P]).then_inc(xt_ready, 1)

            def couple(c, first, last):
                for h in range(2):
                    tile = c * 2 + h
                    if first and h == 0:
                        own = [(n, slot) for kind, n, slot, _ in plan_of(h, first, last) if kind == "own"]
                        act.wait_ge(x_loaded[0], 16)
                        x_high(0, *X0_PARTS[0])
                        w_high(0)
                        x_high(0, *X0_PARTS[1])
                        for part in range(1, len(W_PARTS)):
                            if part <= len(own):
                                evacuate(0, *own[part - 1])
                            w_high(part)
                        act.wait_ge(transposes_ready, len(GROUPS))
                        act.wait_ge(x_loaded[1], 16)
                        x_high(1, 0, FIELDS)
                    for kind, n, slot, _ in plan_of(h, first, last):
                        if kind == "ahead":
                            evacuate(tile + 1, n, slot)
                    if not last:
                        act.wait_ge(scaled, (tile + 1) * PRODUCTS)
                        act.dma_start(x_sb[h][:], x_tiles[c + 1, h]).then_inc(x_loaded[h], 16)
                        act.wait_ge(x_loaded[h], 16 * (c + 2))
                        x_high(h, 0, FIELDS)

            all_couples(act, couple)

        @block.gpsimd
        def _(pool):
            nc.gpsimd.memset(identity[:], 0.0).then_inc(zeroed, 1)
            pool.wait_ge(zeroed, 1)
            nc.gpsimd.affine_select(out=identity[:], in_=identity[:], compare_op=ALU.not_equal, fill=1.0, base=0,
                                    pattern=[[-1, P]], channel_multiplier=1).then_inc(identity_ready, 1)

            def x_low(h, i0, i1):
                nc.gpsimd.tensor_tensor(x_split[:, i0:i1, 1, :],
                                        x_sb[h][:, i0 * E:i1 * E].rearrange("p (i e) -> p i e", e=E),
                                        x_split[:, i0:i1, 0, :], ALU.subtract).then_inc(x_split_ready, 1)

            for n, fields in enumerate(X0_PARTS):
                pool.wait_ge(x_high_ready, n + 1)
                x_low(0, *fields)
            pool.wait_ge(x_split_ready, len(X0_PARTS))
            for n in range(W_LOW_ON_VECTOR, len(W_PARTS)):
                pool.wait_ge(w_high_ready, n + 1)
                cols = pair_cols(*W_PARTS[n])
                nc.gpsimd.tensor_tensor(w_split[E:2 * E, cols], out_sb[0:E, cols], w_split[0:E, cols],
                                        ALU.subtract).then_inc(w_ready[n], 1)
            pool.wait_ge(w_ready[-1], 1)
            pool.wait_ge(x_high_ready, splits(1))
            x_low(1, 0, FIELDS)
            with pool.Fori(1, LAST + 1) as c:
                for h in range(2):
                    pool.wait_ge(x_high_ready, splits(c * 2 + h))
                    x_low(h, 0, FIELDS)

        @block.tensor
        def _(pe):
            def transposes(h, g, slot):
                i0, i1 = GROUPS[g]
                for i in range(i0, i1):
                    for v in range(2):
                        at = ((i - i0) * 2 + v) * P
                        done = nc.tensor.transpose(slots[slot][:, at:at + P],
                                                   x_split[:, i, v:v + 2, :].rearrange("p v e -> p (v e)").bitcast(fp32),
                                                   identity[:])
                done.then_inc(transposes_ready, 1)

            def product(n, slot):
                i, j0, jn = products[n]
                for v in range(2):
                    for a in range(0, jn, BANK_PAIRS):
                        b = min(a + BANK_PAIRS, jn)
                        q = FIRST_PAIR[i] + j0
                        done = nc.tensor.matmul(slots[slot][:, a * E:b * E], xt_sb[:, i, v, :],
                                                w_split[:, (q + a) * E:(q + b) * E], start=(v == 0), stop=(v == 1))
                done.then_inc(product_ready, 1)

            def couple(c, first, last):
                for h in range(2):
                    tile = c * 2 + h
                    for kind, n, slot, before in plan_of(h, first, last):
                        if before:
                            old, m, back = before
                            if old == "product":
                                pe.wait_ge(scaled, (tile + back) * PRODUCTS + m + 1)
                            else:
                                pe.wait_ge(xt_ready, (tile + back + (old == "ahead")) * len(GROUPS) + m + 1)
                        if kind == "product":
                            i, j0, _ = products[n]
                            if j0 == 0 and i in [i0 for i0, _ in GROUPS]:
                                pe.wait_ge(xt_ready, tile * len(GROUPS) + i // GROUP_FIELDS + 1)
                            if first and h == 0 and j0 == 0 and i in [i0 for i0, _ in W_PARTS]:
                                pe.wait_ge(w_ready[[i0 for i0, _ in W_PARTS].index(i)], 1)
                            product(n, slot)
                        elif kind == "own":
                            if n == 0:
                                pe.wait_ge(identity_ready, 1)
                            if n < len(X0_PARTS):
                                pe.wait_ge(x_split_ready, n + 1)
                            transposes(0, n, slot)
                        else:
                            if n == 0:
                                pe.wait_ge(x_split_ready, splits(tile + 1))
                            transposes(1 - h, n, slot)

            all_couples(pe, couple)

        @block.vector
        def _(dve):
            for n in range(W_LOW_ON_VECTOR):
                dve.wait_ge(w_high_ready, n + 1)
                cols = pair_cols(*W_PARTS[n])
                nc.vector.tensor_tensor(w_split[E:2 * E, cols], out_sb[0:E, cols], w_split[0:E, cols],
                                        ALU.subtract).then_inc(w_ready[n], 1)

            def couple(c, first, last):
                for h in range(2):
                    tile = c * 2 + h
                    dve.wait_ge(x_loaded[h], 16 * (c + 1))
                    for kind, n, slot, _ in plan_of(h, first, last):
                        if kind != "product":
                            continue
                        i, j0, jn = products[n]
                        if n in chunk_start and not (first and h == 0):
                            dve.wait_ge(stored[chunk_start.index(n)], 16 * tile)
                        dve.wait_ge(product_ready, tile * PRODUCTS + n + 1)
                        o = (FIRST_PAIR[i] + j0) * E
                        xj = (i + 1 + j0) * E
                        nc.vector.tensor_tensor(out_sb[:, o:o + jn * E], slots[slot][:, 0:jn * E],
                                                x_sb[h][:, xj:xj + jn * E], ALU.mult).then_inc(scaled, 1)

            all_couples(dve, couple)


def kernel(r_x, L0_rec_W):
    import numpy as np
    import concourse.bacc as bacc
    from concourse.bass_utils import run_bass_kernel_spmd

    x = np.ascontiguousarray(r_x)
    w = np.ascontiguousarray(np.transpose(L0_rec_W, (1, 0, 2)))
    B, F, E = x.shape
    fp32 = mybir.dt.float32
    nc = bacc.Bacc("TRN2", target_bir_lowering=False, num_devices=1)
    x_dram = nc.dram_tensor("x_dram", x.shape, fp32, kind="ExternalInput").ap()
    w_dram = nc.dram_tensor("w_dram", w.shape, fp32, kind="ExternalInput").ap()
    out_dram = nc.dram_tensor("out_dram", (B, F * (F - 1) // 2, E), fp32, kind="ExternalOutput").ap()
    pairwise_bilinear(nc, x_dram, w_dram, out_dram)
    result = run_bass_kernel_spmd(nc, [{"x_dram": x, "w_dram": w}], core_ids=[0])
    return result.results[0]["out_dram"]
```

```python
import concourse.bass as bass
from concourse import mybir
from contextlib import ExitStack

P = 128
BANK = 512
SLOT_BANKS = 2
SLOTS = 4


def pairwise_bilinear(nc, x, w, out):
    fp32 = mybir.dt.float32
    fp32r = mybir.dt.float32r
    ALU = mybir.AluOpType
    B, F, E = x.shape
    TILES = B // P
    X_BUFFERS = 4
    FIELDS = F - 1
    PAIRS = F * (F - 1) // 2
    FIRST_PAIR = [i * (2 * F - i - 1) // 2 for i in range(F)]
    BANK_PAIRS = BANK // E
    SLOT_PAIRS = SLOT_BANKS * BANK_PAIRS

    def pair_cols(i0, i1):
        return slice(FIRST_PAIR[i0] * E, FIRST_PAIR[i1] * E)

    products = []
    for i in range(FIELDS):
        partners = F - 1 - i
        n = -(-partners // SLOT_PAIRS)
        cut = [partners * c // n for c in range(n + 1)]
        products += [(i, a, b - a) for a, b in zip(cut, cut[1:])]
    PRODUCTS = len(products)

    GROUP_FIELDS = SLOT_BANKS * BANK // (2 * P)
    GROUPS = [(f, min(f + GROUP_FIELDS, FIELDS)) for f in range(0, FIELDS, GROUP_FIELDS)]
    AHEAD_AFTER = [9, 11, 13, 15, 19, FIELDS - 1]
    OWN_BEFORE = [0, 2, 3, 4, 4, 4]

    assert all(AHEAD_AFTER[g] >= i1 - 1 for g, (_, i1) in enumerate(GROUPS))
    assert all(OWN_BEFORE[g] <= i0 for g, (i0, _) in enumerate(GROUPS))

    def uses_of(first, last):
        uses = []
        for i in range(FIELDS):
            if first:
                uses += [("own", g) for g in range(len(GROUPS)) if OWN_BEFORE[g] == i]
            uses += [("product", n) for n, piece in enumerate(products) if piece[0] == i]
            if not last:
                uses += [("ahead", g) for g in range(len(GROUPS)) if AHEAD_AFTER[g] == i]
        return uses

    assert len(uses_of(False, False)) % SLOTS == 0

    def plan(first, last):
        uses = uses_of(first, last)
        start = -len(uses) if first else 0
        holder = {}
        if not first:
            holder = {u % SLOTS: (*use, -1) for u, use in enumerate(uses_of(False, False))}
        planned = []
        for u, use in enumerate(uses):
            slot = (start + u) % SLOTS
            planned.append((*use, slot, holder.get(slot)))
            holder[slot] = (*use, 0)
        return planned

    CHUNKS = [(0, 2), (2, 4), (4, 6), (6, 8), (8, 10), (10, 12), (12, 15), (15, FIELDS)]
    chunk_start = [min(n for n, piece in enumerate(products) if piece[0] >= i0) for i0, _ in CHUNKS]
    chunk_end = chunk_start[1:] + [PRODUCTS]
    W_PARTS = [(0, 1), (1, 2)] + CHUNKS[1:]
    W_ON_VECTOR = {0: [0, 1], 1: [3], 4: [5]}
    W_ON_OTHERS = [n for n in range(len(W_PARTS)) if n not in sum(W_ON_VECTOR.values(), [])]

    x_tiles = x.rearrange("(t p) f e -> t p (f e)", p=P)
    out_tiles = out.rearrange("(t p) q e -> t p (q e)", p=P)
    w_cols = w.rearrange("e q f -> e (q f)")

    with ExitStack() as ctx:
        def sb(name, shape, dt=fp32):
            return ctx.enter_context(nc.sbuf_tensor(name, shape, dt))

        def sem(name):
            return ctx.enter_context(nc.semaphore(name))

        w_split = sb("w_split", [P, PAIRS * E], fp32r)
        x_sb = [sb(f"x_sb{n}", [P, F * E]) for n in range(X_BUFFERS)]
        x_split = sb("x_split", [P, FIELDS, 3, E], fp32r)
        xt_sb = sb("xt_sb", [P, FIELDS, 2, P], fp32r)
        out_sb = sb("out_sb", [P, PAIRS * E])
        identity = sb("identity", [P, P])
        slots = [ctx.enter_context(nc.psum_tensor(f"slot{s}", [P, SLOT_BANKS * BANK], fp32)) for s in range(SLOTS)]

        zeroed = sem("zeroed")
        identity_ready = sem("identity_ready")
        w_loaded = [sem(f"w_loaded{n}") for n in range(len(W_PARTS))]
        w_high_ready = sem("w_high_ready")
        w_high_vector = sem("w_high_vector")
        w_ready = [sem(f"w_ready{n}") for n in range(len(W_PARTS))]
        x_loaded = [sem(f"x_loaded{n}") for n in range(X_BUFFERS)]
        x_high_ready = sem("x_high_ready")
        x_split_ready = sem("x_split_ready")
        transposes_ready = sem("transposes_ready")
        xt_ready = sem("xt_ready")
        product_ready = sem("product_ready")
        scaled = sem("scaled")
        stored = [sem(f"stored{c}") for c in range(len(CHUNKS))]

        block = ctx.enter_context(nc.Block())

        X0_PARTS = [GROUPS[0], (GROUPS[0][1], FIELDS)]

        def splits(tile):
            return tile + len(X0_PARTS)

        def number(c, s):
            return c * X_BUFFERS + s

        def loads(c, s):
            return c + s // X_BUFFERS + 1

        def all_tiles(eng, program):
            ahead = X_BUFFERS - 1
            program(0, 0, True, ahead)
            rounds = (TILES - 1) // X_BUFFERS
            with eng.Fori(0, rounds) as c:
                for s in range(1, X_BUFFERS + 1):
                    program(c, s, False, ahead)
            for s in range(1, TILES - rounds * X_BUFFERS):
                program(rounds, s, False, TILES - 1 - number(rounds, s))

        assert TILES % X_BUFFERS == 0

        @block.sync
        def _(sp):
            for n, (i0, i1) in enumerate(W_PARTS):
                cols = pair_cols(i0, i1)
                sp.dma_start(out_sb[0:E, cols], w_cols[:, cols]).then_inc(w_loaded[n], 16)

            def store(c, s, first, left):
                tile = number(c, s)
                for n, (i0, i1) in enumerate(CHUNKS):
                    sp.wait_ge(scaled, tile * PRODUCTS + chunk_end[n])
                    cols = pair_cols(i0, i1)
                    sp.dma_start(out_tiles[tile, :, cols], out_sb[:, cols]).then_inc(stored[n], 16)

            all_tiles(sp, store)
            for n in range(len(CHUNKS)):
                sp.wait_ge(stored[n], 16 * TILES)

        @block.scalar
        def _(act):
            def load_x(c, s):
                act.dma_start(x_sb[s % X_BUFFERS][:], x_tiles[number(c, s)]).then_inc(x_loaded[s % X_BUFFERS], 16)

            def x_high(c, s, i0, i1):
                act.wait_ge(x_loaded[s % X_BUFFERS], 16 * loads(c, s))
                nc.scalar.copy(x_split[:, i0:i1, 0:3:2, :],
                               x_sb[s % X_BUFFERS][:, i0 * E:i1 * E].rearrange("p (i o e) -> p i o e", o=1, e=E)
                               .to_broadcast([P, i1 - i0, 2, E])).then_inc(x_high_ready, 1)

            def w_high(n):
                act.wait_ge(w_loaded[n], 16)
                cols = pair_cols(*W_PARTS[n])
                nc.scalar.copy(w_split[0:E, cols], out_sb[0:E, cols]).then_inc(w_high_ready, 1)

            def evacuate(tile, g, slot):
                i0, i1 = GROUPS[g]
                act.wait_ge(transposes_ready, tile * len(GROUPS) + g + 1)
                nc.scalar.copy(xt_sb[:, i0:i1].rearrange("p i v b -> p (i v b)"),
                               slots[slot][:, 0:(i1 - i0) * 2 * P]).then_inc(xt_ready, 1)

            def tile_program(c, s, first, left):
                tile = number(c, s)
                planned = plan(first, left == 0)
                if first:
                    own = [(n, slot) for kind, n, slot, _ in planned if kind == "own"]
                    load_x(0, 0)
                    x_high(0, 0, *X0_PARTS[0])
                    x_high(0, 0, *X0_PARTS[1])
                    evacuate(0, *own[0])
                    w_high(W_ON_OTHERS[0])
                    load_x(0, 1)
                    for n, slot in own[1:2]:
                        evacuate(0, n, slot)
                    w_high(W_ON_OTHERS[1])
                    for n, slot in own[2:]:
                        evacuate(0, n, slot)
                    load_x(0, 2)
                    w_high(W_ON_OTHERS[2])
                    x_high(0, 1, 0, FIELDS)
                    for n in W_ON_OTHERS[3:]:
                        w_high(n)
                if left >= 3:
                    if not first:
                        act.wait_ge(scaled, tile * PRODUCTS)
                    load_x(c, s + 3)
                for kind, n, slot, _ in planned:
                    if kind == "ahead":
                        evacuate(tile + 1, n, slot)
                if left >= 2:
                    x_high(c, s + 2, 0, FIELDS)

            all_tiles(act, tile_program)

        @block.gpsimd
        def _(pool):
            nc.gpsimd.memset(identity[:], 0.0).then_inc(zeroed, 1)
            pool.wait_ge(zeroed, 1)
            nc.gpsimd.affine_select(out=identity[:], in_=identity[:], compare_op=ALU.not_equal, fill=1.0, base=0,
                                    pattern=[[-1, P]], channel_multiplier=1).then_inc(identity_ready, 1)

            def x_low(s, i0, i1):
                nc.gpsimd.tensor_tensor(x_split[:, i0:i1, 1, :],
                                        x_sb[s % X_BUFFERS][:, i0 * E:i1 * E].rearrange("p (i e) -> p i e", e=E),
                                        x_split[:, i0:i1, 0, :], ALU.subtract).then_inc(x_split_ready, 1)

            for n, fields in enumerate(X0_PARTS):
                pool.wait_ge(x_high_ready, n + 1)
                x_low(0, *fields)

            def w_low(k):
                n = W_ON_OTHERS[k]
                pool.wait_ge(w_high_ready, k + 1)
                cols = pair_cols(*W_PARTS[n])
                nc.gpsimd.tensor_tensor(w_split[E:2 * E, cols], out_sb[0:E, cols], w_split[0:E, cols],
                                        ALU.subtract).then_inc(w_ready[n], 1)

            pool.wait_ge(x_split_ready, len(X0_PARTS))
            for k in range(3):
                w_low(k)
            pool.wait_ge(w_ready[W_ON_OTHERS[2]], 1)
            pool.wait_ge(x_high_ready, splits(1))
            x_low(1, 0, FIELDS)
            pool.wait_ge(x_split_ready, splits(1))
            for k in range(3, len(W_ON_OTHERS)):
                w_low(k)
            pool.wait_ge(w_ready[W_ON_OTHERS[-1]], 1)

            def tile_program(c, s, first, left):
                if left >= 2:
                    pool.wait_ge(x_high_ready, splits(number(c, s + 2)))
                    x_low(s + 2, 0, FIELDS)

            all_tiles(pool, tile_program)

        @block.tensor
        def _(pe):
            def transposes(g, slot):
                i0, i1 = GROUPS[g]
                for i in range(i0, i1):
                    for v in range(2):
                        at = ((i - i0) * 2 + v) * P
                        done = nc.tensor.transpose(slots[slot][:, at:at + P],
                                                   x_split[:, i, v:v + 2, :].rearrange("p v e -> p (v e)").bitcast(fp32),
                                                   identity[:])
                done.then_inc(transposes_ready, 1)

            def product(n, slot):
                i, j0, jn = products[n]
                for v in range(2):
                    for a in range(0, jn, BANK_PAIRS):
                        b = min(a + BANK_PAIRS, jn)
                        q = FIRST_PAIR[i] + j0
                        done = nc.tensor.matmul(slots[slot][:, a * E:b * E], xt_sb[:, i, v, :],
                                                w_split[:, (q + a) * E:(q + b) * E], start=(v == 0), stop=(v == 1))
                done.then_inc(product_ready, 1)

            def tile_program(c, s, first, left):
                tile = number(c, s)
                for kind, n, slot, before in plan(first, left == 0):
                    if before:
                        old, m, back = before
                        if old == "product":
                            pe.wait_ge(scaled, (tile + back) * PRODUCTS + m + 1)
                        else:
                            pe.wait_ge(xt_ready, (tile + back + (old == "ahead")) * len(GROUPS) + m + 1)
                    if kind == "product":
                        i, j0, _ = products[n]
                        if j0 == 0 and i in [i0 for i0, _ in GROUPS]:
                            pe.wait_ge(xt_ready, tile * len(GROUPS) + i // GROUP_FIELDS + 1)
                        if first and j0 == 0 and i in [i0 for i0, _ in W_PARTS]:
                            pe.wait_ge(w_ready[[i0 for i0, _ in W_PARTS].index(i)], 1)
                        product(n, slot)
                    elif kind == "own":
                        if n == 0:
                            pe.wait_ge(identity_ready, 1)
                        if n < len(X0_PARTS):
                            pe.wait_ge(x_split_ready, n + 1)
                        transposes(n, slot)
                    else:
                        if n == 0:
                            pe.wait_ge(x_split_ready, splits(tile + 1))
                        transposes(n, slot)

            all_tiles(pe, tile_program)

        @block.vector
        def _(dve):
            def split_w(n):
                dve.wait_ge(w_loaded[n], 16)
                cols = pair_cols(*W_PARTS[n])
                nc.vector.tensor_copy(w_split[0:E, cols], out_sb[0:E, cols]).then_inc(w_high_vector, 1)
                dve.wait_ge(w_high_vector, sum(W_ON_VECTOR.values(), []).index(n) + 1)
                nc.vector.tensor_tensor(w_split[E:2 * E, cols], out_sb[0:E, cols], w_split[0:E, cols],
                                        ALU.subtract).then_inc(w_ready[n], 1)

            def tile_program(c, s, first, left):
                tile = number(c, s)
                x_tile = x_sb[s % X_BUFFERS]
                for kind, n, slot, _ in plan(first, left == 0):
                    if kind != "product":
                        continue
                    i, j0, jn = products[n]
                    if first and j0 == 0:
                        for part in W_ON_VECTOR.get(i, []):
                            split_w(part)
                    if n in chunk_start and not first:
                        dve.wait_ge(stored[chunk_start.index(n)], 16 * tile)
                    if n == 0:
                        dve.wait_ge(x_loaded[s % X_BUFFERS], 16 * loads(c, s))
                    dve.wait_ge(product_ready, tile * PRODUCTS + n + 1)
                    o = (FIRST_PAIR[i] + j0) * E
                    xj = (i + 1 + j0) * E
                    nc.vector.tensor_tensor(out_sb[:, o:o + jn * E], slots[slot][:, 0:jn * E],
                                            x_tile[:, xj:xj + jn * E], ALU.mult).then_inc(scaled, 1)

            all_tiles(dve, tile_program)


def kernel(r_x, L0_rec_W):
    import numpy as np
    import concourse.bacc as bacc
    from concourse.bass_utils import run_bass_kernel_spmd

    x = np.ascontiguousarray(r_x)
    w = np.ascontiguousarray(np.transpose(L0_rec_W, (1, 0, 2)))
    B, F, E = x.shape
    fp32 = mybir.dt.float32
    nc = bacc.Bacc("TRN2", target_bir_lowering=False, num_devices=1)
    x_dram = nc.dram_tensor("x_dram", x.shape, fp32, kind="ExternalInput").ap()
    w_dram = nc.dram_tensor("w_dram", w.shape, fp32, kind="ExternalInput").ap()
    out_dram = nc.dram_tensor("out_dram", (B, F * (F - 1) // 2, E), fp32, kind="ExternalOutput").ap()
    pairwise_bilinear(nc, x_dram, w_dram, out_dram)
    result = run_bass_kernel_spmd(nc, [{"x_dram": x, "w_dram": w}], core_ids=[0])
    return result.results[0]["out_dram"]
```
